# Optimizing a Trainium2 kernel written in Bass

```python
import numpy as np
import jax
import jax.numpy as jnp

def _softmax(x, axis=-1):
    return jax.nn.softmax(x, axis=axis)

def _gelu(x):
    return jax.nn.gelu(x, approximate=True)

def _silu(x):
    return jax.nn.silu(x)

def _sigmoid(x):
    return jax.nn.sigmoid(x)

def _layernorm(x, axis=-1, eps=1e-05):
    m = jnp.mean(x, axis=axis, keepdims=True)
    v = jnp.var(x, axis=axis, keepdims=True)
    return (x - m) / jnp.sqrt(v + eps)

def _scatter_add(tgt, idx, src, axis=0):
    return tgt.at[idx].add(src)

def _segment_sum(src, seg, n):
    return jax.ops.segment_sum(src, seg, n)
kernel_name = 'mk_vit_tower_d2_tok_img1024_r4_71044e'

def setup_inputs(seed: int=0):
    np.random.seed(seed)
    _w = jnp.asarray

    def _rec_inputs():
        import jax
        import jax.numpy as jnp
        _rk = jax.random.key(seed)
        x = -0.00016672 + 0.999947 * jax.random.normal(jax.random.fold_in(_rk, 1), (16, 3, 96, 96), jnp.float32)
        return x
    x = _rec_inputs()

    def _L0_tok_setup():
        import jax, jax.numpy as jnp
        import numpy as np
        IMAGE_SIZE = 96
        PATCH = 16
        N_EMBD = 256
        C = 3
        N_PATCHES = (IMAGE_SIZE // PATCH) ** 2
        PATCH_DIM = C * PATCH * PATCH
        key = jax.random.key(seed)
        kx, kw, kb, kp = jax.random.split(key, 4)
        B = 64
        x = jax.random.normal(kx, (B, C, IMAGE_SIZE, IMAGE_SIZE), dtype=jnp.float32)
        bound = 1.0 / np.sqrt(PATCH_DIM)
        W = jax.random.uniform(kw, (N_EMBD, PATCH_DIM), minval=-bound, maxval=bound, dtype=jnp.float32)
        b = jax.random.uniform(kb, (N_EMBD,), minval=-bound, maxval=bound, dtype=jnp.float32)
        pos_embd = jax.random.normal(kp, (1, N_PATCHES, N_EMBD), dtype=jnp.float32) * 0.02
        return {'x': x, 'W': W, 'b': b, 'pos_embd': pos_embd}
    _L0_tok_all = _L0_tok_setup()
    _L0_tok_in = {k: v for k, v in _L0_tok_all.items() if k in ('W', 'b', 'pos_embd')}
    del _L0_tok_all

    def _L0_attn_setup():
        import jax, jax.numpy as jnp
        import numpy as np
        EMBED_DIM = 256
        NUM_HEADS = 16
        HEAD_DIM = EMBED_DIM // NUM_HEADS
        FEATURE_EPS = 1e-06
        DEN_EPS = 1e-06
        key = jax.random.key(seed)
        k_x, k_qw, k_qb, k_ow, k_ob = jax.random.split(key, 5)
        b, l = (2, 512)
        x = jax.random.normal(k_x, (b, l, EMBED_DIM), dtype=jnp.float32)
        s = 1.0 / np.sqrt(EMBED_DIM)
        qkv_w = jax.random.uniform(k_qw, (3 * EMBED_DIM, EMBED_DIM), minval=-s, maxval=s, dtype=jnp.float32)
        qkv_b = jax.random.uniform(k_qb, (3 * EMBED_DIM,), minval=-s, maxval=s, dtype=jnp.float32)
        out_w = jax.random.uniform(k_ow, (EMBED_DIM, EMBED_DIM), minval=-s, maxval=s, dtype=jnp.float32)
        out_b = jax.random.uniform(k_ob, (EMBED_DIM,), minval=-s, maxval=s, dtype=jnp.float32)
        return {'x': x, 'qkv_w': qkv_w, 'qkv_b': qkv_b, 'out_w': out_w, 'out_b': out_b}
    _L0_attn_all = _L0_attn_setup()
    _L0_attn_in = {k: v for k, v in _L0_attn_all.items() if k in ('qkv_w', 'qkv_b', 'out_w', 'out_b')}
    del _L0_attn_all

    def _L0_ffn_setup():
        import jax, jax.numpy as jnp
        import numpy as np
        B, S, D_MODEL, D_HIDDEN = (4, 512, 256, 1024)

        def act_quant(x):
            scale = 127.0 / jnp.clip(jnp.max(jnp.abs(x), axis=-1, keepdims=True), 1e-05)
            return jnp.clip(jnp.round(x * scale), -128, 127) / scale

        def weight_quant(w):
            scale = 1.0 / jnp.clip(jnp.mean(jnp.abs(w)), 1e-05)
            return jnp.clip(jnp.round(w * scale), -1, 1) / scale

        def bit_linear(x, w):
            xq = x + jax.lax.stop_gradient(act_quant(x) - x)
            wq = w + jax.lax.stop_gradient(weight_quant(w) - w)
            return jnp.einsum('bsd,hd->bsh', xq, wq)

        def depthwise_conv1d(x_bcl, w, b):
            y = jax.lax.conv_general_dilated(x_bcl, w, window_strides=(1,), padding=[(1, 1)], dimension_numbers=('NCH', 'OIH', 'NCH'), feature_group_count=x_bcl.shape[1])
            return y + b[None, :, None]
        key = jax.random.key(seed)
        ks = jax.random.split(key, 5)
        lim1 = 1.0 / np.sqrt(D_MODEL)
        lim2 = 1.0 / np.sqrt(D_HIDDEN)
        limc = 1.0 / np.sqrt(3.0)
        return {'x': jax.random.normal(ks[0], (B, S, D_MODEL), dtype=jnp.float32), 'w1': jax.random.uniform(ks[1], (D_HIDDEN, D_MODEL), jnp.float32, -lim1, lim1), 'conv_w': jax.random.uniform(ks[2], (D_HIDDEN, 1, 3), jnp.float32, -limc, limc), 'conv_b': jax.random.uniform(ks[3], (D_HIDDEN,), jnp.float32, -limc, limc), 'w2': jax.random.uniform(ks[4], (D_MODEL, D_HIDDEN), jnp.float32, -lim2, lim2)}
    _L0_ffn_all = _L0_ffn_setup()
    _L0_ffn_in = {k: v for k, v in _L0_ffn_all.items() if k in ('w1', 'conv_w', 'conv_b', 'w2')}
    del _L0_ffn_all

    def _L1_attn_setup():
        import jax, jax.numpy as jnp
        import numpy as np
        from math import sqrt
        HEADS = 16
        MODEL_DIM = 256
        DIM_PER_HEAD = MODEL_DIM // HEADS
        MAX_REL_POS = 32
        ROPE_BASE = 10000.0
        NEG_INF = -1e+18

        def _rope_cos_sin(seq_len, dim):
            inv_freq = 1.0 / ROPE_BASE ** (jnp.arange(0, dim, 2, dtype=jnp.float32) / dim)
            t = jnp.arange(seq_len, dtype=jnp.float32)
            ang = jnp.outer(t, inv_freq)
            return (jnp.cos(ang), jnp.sin(ang))

        def _apply_rotary_interleave(x, cos, sin):
            B, H, L, D = x.shape
            x_ = x.reshape(B, H, L, D // 2, 2)
            xe, xo = (x_[..., 0], x_[..., 1])
            c = cos[None, None, :, :]
            s = sin[None, None, :, :]
            oe = xe * c - xo * s
            oo = xe * s + xo * c
            return jnp.stack([oe, oo], axis=-1).reshape(B, H, L, D)
        key = jax.random.key(seed)
        ks = jax.random.split(key, 6)
        B, L = (2, 256)
        scale = 0.02
        x = jax.random.normal(ks[0], (B, L, MODEL_DIM), dtype=jnp.float32)
        w_q = jax.random.normal(ks[1], (MODEL_DIM, MODEL_DIM), dtype=jnp.float32) * scale
        w_k = jax.random.normal(ks[2], (MODEL_DIM, MODEL_DIM), dtype=jnp.float32) * scale
        w_v = jax.random.normal(ks[3], (MODEL_DIM, MODEL_DIM), dtype=jnp.float32) * scale
        w_o = jax.random.normal(ks[4], (MODEL_DIM, MODEL_DIM), dtype=jnp.float32) * scale
        rel_emb = jax.random.normal(ks[5], (2 * MAX_REL_POS + 1, DIM_PER_HEAD), dtype=jnp.float32) * scale
        return {'x': x, 'w_q': w_q, 'w_k': w_k, 'w_v': w_v, 'w_o': w_o, 'rel_emb': rel_emb}
    _L1_attn_all = _L1_attn_setup()
    _L1_attn_in = {k: v for k, v in _L1_attn_all.items() if k in ('w_q', 'w_k', 'w_v', 'w_o', 'rel_emb')}
    del _L1_attn_all

    def _L1_ffn_setup():
        import jax, jax.numpy as jnp
        import numpy as np
        B, S, D, O, E, R, TOP_K = (4, 256, 256, 256, 8, 16, 2)
        SCALING = 32.0 / 16.0
        NEG_INF = -1000000000.0
        key = jax.random.key(seed)
        ks = jax.random.split(key, 6)
        return {'x': jax.random.normal(ks[0], (B, S, D), jnp.float32), 'base_w': jax.random.normal(ks[1], (O, D), jnp.float32) * 0.02, 'base_b': jnp.zeros((O,), jnp.float32), 'lora_A': jax.random.normal(ks[2], (E, D, R), jnp.float32) * 0.02, 'lora_B': jax.random.normal(ks[3], (E, R, O), jnp.float32) * 0.02, 'router_w': jax.random.normal(ks[4], (E, D), jnp.float32) * 0.02, 'router_b': jnp.zeros((E,), jnp.float32)}
    _L1_ffn_all = _L1_ffn_setup()
    _L1_ffn_in = {k: v for k, v in _L1_ffn_all.items() if k in ('base_w', 'base_b', 'lora_A', 'lora_B', 'router_w', 'router_b')}
    del _L1_ffn_all
    return {'x': x, 'L0_tok_W': _L0_tok_in['W'], 'L0_tok_b': _L0_tok_in['b'], 'L0_tok_pos_embd': _L0_tok_in['pos_embd'], 'L0_attn_qkv_w': _L0_attn_in['qkv_w'], 'L0_attn_qkv_b': _L0_attn_in['qkv_b'], 'L0_attn_out_w': _L0_attn_in['out_w'], 'L0_attn_out_b': _L0_attn_in['out_b'], 'L0_ffn_w1': _L0_ffn_in['w1'], 'L0_ffn_conv_w': _L0_ffn_in['conv_w'], 'L0_ffn_conv_b': _L0_ffn_in['conv_b'], 'L0_ffn_w2': _L0_ffn_in['w2'], 'L1_attn_w_q': _L1_attn_in['w_q'], 'L1_attn_w_k': _L1_attn_in['w_k'], 'L1_attn_w_v': _L1_attn_in['w_v'], 'L1_attn_w_o': _L1_attn_in['w_o'], 'L1_attn_rel_emb': _L1_attn_in['rel_emb'], 'L1_ffn_base_w': _L1_ffn_in['base_w'], 'L1_ffn_base_b': _L1_ffn_in['base_b'], 'L1_ffn_lora_A': _L1_ffn_in['lora_A'], 'L1_ffn_lora_B': _L1_ffn_in['lora_B'], 'L1_ffn_router_w': _L1_ffn_in['router_w'], 'L1_ffn_router_b': _L1_ffn_in['router_b']}

def reference(x, L0_tok_W, L0_tok_b, L0_tok_pos_embd, L0_attn_qkv_w, L0_attn_qkv_b, L0_attn_out_w, L0_attn_out_b, L0_ffn_w1, L0_ffn_conv_w, L0_ffn_conv_b, L0_ffn_w2, L1_attn_w_q, L1_attn_w_k, L1_attn_w_v, L1_attn_w_o, L1_attn_rel_emb, L1_ffn_base_w, L1_ffn_base_b, L1_ffn_lora_A, L1_ffn_lora_B, L1_ffn_router_w, L1_ffn_router_b):
    import jax
    import jax.numpy as jnp

    def _L0_tok_ref(x, W, b, pos_embd):
        import jax, jax.numpy as jnp
        import numpy as np
        IMAGE_SIZE = 96
        PATCH = 16
        N_EMBD = 256
        C = 3
        N_PATCHES = (IMAGE_SIZE // PATCH) ** 2
        PATCH_DIM = C * PATCH * PATCH
        B, Cc, H, Wd = x.shape
        p = PATCH
        Hp, Wp = (H // p, Wd // p)
        patches = x.reshape(B, Cc, Hp, p, Wp, p)
        patches = patches.transpose(0, 2, 4, 1, 3, 5)
        patches = patches.reshape(B, Hp * Wp, Cc * p * p)
        out = jnp.einsum('bnd,ed->bne', patches, W) + b + pos_embd
        return out

    def _L0_attn_ref(x, qkv_w, qkv_b, out_w, out_b):
        import jax, jax.numpy as jnp
        import numpy as np
        EMBED_DIM = 256
        NUM_HEADS = 16
        HEAD_DIM = EMBED_DIM // NUM_HEADS
        FEATURE_EPS = 1e-06
        DEN_EPS = 1e-06
        b, l, e = x.shape
        qkv = (x @ qkv_w.T + qkv_b).reshape(b, l, 3, NUM_HEADS, HEAD_DIM)
        qkv = jnp.transpose(qkv, (2, 0, 3, 1, 4))
        q, k, v = (qkv[0], qkv[1], qkv[2])
        q = jax.nn.relu(q) + FEATURE_EPS
        k = jax.nn.relu(k) + FEATURE_EPS
        kv = jnp.cumsum(jnp.einsum('bhld,bhle->bhlde', k, v), axis=2)
        k_cum = jnp.cumsum(k, axis=2)
        num = jnp.einsum('bhld,bhlde->bhle', q, kv)
        den = jnp.maximum(jnp.einsum('bhld,bhld->bhl', q, k_cum)[..., None], DEN_EPS)
        out = num / den
        out = jnp.transpose(out, (0, 2, 1, 3)).reshape(b, l, e)
        return out @ out_w.T + out_b

    def _L0_ffn_ref(x, w1, conv_w, conv_b, w2):
        import jax, jax.numpy as jnp
        import numpy as np
        B, S, D_MODEL, D_HIDDEN = (4, 512, 256, 1024)

        def act_quant(x):
            scale = 127.0 / jnp.clip(jnp.max(jnp.abs(x), axis=-1, keepdims=True), 1e-05)
            return jnp.clip(jnp.round(x * scale), -128, 127) / scale

        def weight_quant(w):
            scale = 1.0 / jnp.clip(jnp.mean(jnp.abs(w)), 1e-05)
            return jnp.clip(jnp.round(w * scale), -1, 1) / scale

        def bit_linear(x, w):
            xq = x + jax.lax.stop_gradient(act_quant(x) - x)
            wq = w + jax.lax.stop_gradient(weight_quant(w) - w)
            return jnp.einsum('bsd,hd->bsh', xq, wq)

        def depthwise_conv1d(x_bcl, w, b):
            y = jax.lax.conv_general_dilated(x_bcl, w, window_strides=(1,), padding=[(1, 1)], dimension_numbers=('NCH', 'OIH', 'NCH'), feature_group_count=x_bcl.shape[1])
            return y + b[None, :, None]
        h = bit_linear(x, w1)
        h = depthwise_conv1d(h.transpose(0, 2, 1), conv_w, conv_b)
        h = h.transpose(0, 2, 1)
        h = jax.nn.silu(h)
        return bit_linear(h, w2)

    def _L1_attn_ref(x, w_q, w_k, w_v, w_o, rel_emb):
        import jax, jax.numpy as jnp
        import numpy as np
        from math import sqrt
        HEADS = 16
        MODEL_DIM = 256
        DIM_PER_HEAD = MODEL_DIM // HEADS
        MAX_REL_POS = 32
        ROPE_BASE = 10000.0
        NEG_INF = -1e+18

        def _rope_cos_sin(seq_len, dim):
            inv_freq = 1.0 / ROPE_BASE ** (jnp.arange(0, dim, 2, dtype=jnp.float32) / dim)
            t = jnp.arange(seq_len, dtype=jnp.float32)
            ang = jnp.outer(t, inv_freq)
            return (jnp.cos(ang), jnp.sin(ang))

        def _apply_rotary_interleave(x, cos, sin):
            B, H, L, D = x.shape
            x_ = x.reshape(B, H, L, D // 2, 2)
            xe, xo = (x_[..., 0], x_[..., 1])
            c = cos[None, None, :, :]
            s = sin[None, None, :, :]
            oe = xe * c - xo * s
            oo = xe * s + xo * c
            return jnp.stack([oe, oo], axis=-1).reshape(B, H, L, D)
        B, L, _ = x.shape

        def shape(t):
            return t.reshape(B, L, HEADS, DIM_PER_HEAD).transpose(0, 2, 1, 3)
        q = shape(x @ w_q.T)
        k = shape(x @ w_k.T)
        v = shape(x @ w_v.T)
        cos, sin = _rope_cos_sin(L, DIM_PER_HEAD)
        q = _apply_rotary_interleave(q, cos, sin)
        k = _apply_rotary_interleave(k, cos, sin)
        q = q / sqrt(DIM_PER_HEAD)
        scores = jnp.einsum('bhqd,bhkd->bhqk', q, k)
        pos = jnp.arange(L)
        rel_idx = jnp.clip(pos[None, :] - pos[:, None], -MAX_REL_POS, MAX_REL_POS) + MAX_REL_POS
        rel = rel_emb[rel_idx]
        scores = scores + jnp.einsum('bhqd,qkd->bhqk', q, rel)
        causal = jnp.tril(jnp.ones((L, L), dtype=bool))
        scores = jnp.where(causal[None, None], scores, NEG_INF)
        attn = jax.nn.softmax(scores, axis=-1)
        ctx = jnp.einsum('bhqk,bhkd->bhqd', attn, v)
        ctx = ctx + jnp.einsum('bhqk,qkd->bhqd', attn, rel)
        out = ctx.transpose(0, 2, 1, 3).reshape(B, L, MODEL_DIM) @ w_o.T
        return out

    def _L1_ffn_ref(x, base_w, base_b, lora_A, lora_B, router_w, router_b):
        import jax, jax.numpy as jnp
        import numpy as np
        B, S, D, O, E, R, TOP_K = (4, 256, 256, 256, 8, 16, 2)
        SCALING = 32.0 / 16.0
        NEG_INF = -1000000000.0
        result = jnp.einsum('bsd,od->bso', x, base_w) + base_b
        ax = jnp.einsum('bsd,edr->bser', x, lora_A)
        bax = jnp.einsum('bser,ero->bseo', ax, lora_B)
        logits = jnp.einsum('bsd,ed->bse', x, router_w) + router_b
        kth = jax.lax.top_k(logits, TOP_K)[0][..., -1:]
        masked = jnp.where(logits < kth, NEG_INF, logits)
        expert_weights = jax.nn.softmax(masked, axis=-1)
        return result + SCALING * jnp.einsum('bse,bseo->bso', expert_weights, bax)
    h = _L0_tok_ref(x, L0_tok_W, L0_tok_b, L0_tok_pos_embd)
    h = h + _L0_attn_ref(_layernorm(h, axis=-1), L0_attn_qkv_w, L0_attn_qkv_b, L0_attn_out_w, L0_attn_out_b)
    h = h + _L0_ffn_ref(_layernorm(h, axis=-1), L0_ffn_w1, L0_ffn_conv_w, L0_ffn_conv_b, L0_ffn_w2)
    h = h + _L1_attn_ref(_layernorm(h, axis=-1), L1_attn_w_q, L1_attn_w_k, L1_attn_w_v, L1_attn_w_o, L1_attn_rel_emb)
    h = h + _L1_ffn_ref(_layernorm(h, axis=-1), L1_ffn_base_w, L1_ffn_base_b, L1_ffn_lora_A, L1_ffn_lora_B, L1_ffn_router_w, L1_ffn_router_b)
    return h

_drawn_inputs = setup_inputs


def setup_inputs(seed=0):
    import zlib

    import numpy as np

    out = dict(_drawn_inputs(seed))
    spreads = {'L1_ffn_base_b': (0.0, 0.1), 'L1_ffn_router_b': (0.0, 0.283)}
    factors = {'L1_attn_w_q': 8.0, 'L1_attn_w_k': 8.0, 'L1_attn_rel_emb': 8.0}
    for name, (base, spread) in spreads.items():
        noise = np.random.default_rng([zlib.crc32(name.encode()), seed]).standard_normal(out[name].shape)
        drawn = base * np.exp(spread * noise) if base else spread * noise
        out[name] = jnp.asarray(drawn.astype(out[name].dtype))
    for name, factor in factors.items():
        out[name] = (out[name] * factor).astype(out[name].dtype)
    return out
```

```python
from contextlib import ExitStack

import numpy as np

import concourse.bass as bass
from concourse import mybir

ALU = mybir.AluOpType
ACT = mybir.ActivationFunctionType
AX = mybir.AxisListType
F32 = mybir.dt.float32
BF16 = mybir.dt.bfloat16

B, L, D, H, E = 16, 36, 256, 16, 16
P = 128
SLOT = 64
ROWS = SLOT + L
KD = D // P
HC = H // KD
PATCH = 768
KP = PATCH // P
HID = 1024
MH = HID // P
HALF = B // 2
NT = HALF // 2
TOK = HALF * L
TILES = B // 2
VW = E + 1
SEL = [(0, 3), (3, 6), (6, 8)]
G3 = 3 * L
ZROW = (2 * L - 1) * H
EXPERTS, RANK = 8, 16
FA = D + EXPERTS * RANK + EXPERTS
LN_EPS = 1e-5
FEATURE_EPS = 1e-6
DEN_EPS = 1e-6
QUANT_EPS = 1e-5
NEG = -1e18
ROUND = 1.5 * 2.0 ** 23
QMAX = 127.0
LORA_SCALE = 2.0

STAGES = ["embed", "norm0", "proj0", "weights", "score0", "sum0", "out0", "norm1", "conv", "ffn0", "norm2", "proj1", "score1",
          "sum1", "out1", "norm3", "ffn1"]
ORDER = [(s, h) for s in STAGES for h in ((0,) if s == "weights" else (0, 1))]
LN_AT = {(int(s[-1]), h): n + 1 for n, (s, h) in enumerate(x for x in ORDER if x[0].startswith("norm"))}

PRODUCTS = {
    "embed": [("embed", KD, "h0f_ready"), ("h0t", 2, "h0_ready")],
    "norm0": [("xt0", KD, "xf0_ready")],
    "weights": [("wsum", 1, "wscale_ready")],
    "proj0": [("qk0", 2 * KD, "qk0_ready"), ("v0", 2, "v2_ready")],
    "score0": [("s0", 2 * NT, "st_ready")],
    "sum0": [("pv0", 4, "a0_ready"), ("at0", KD, "af0_ready")],
    "out0": [("o0", 2, "h1_ready")],
    "norm1": [("xt1", 1, "xqf_ready"), ("sb1", 1, "sb1_ready")],
    "conv": [("f1", MH, "g_ready")],
    "ffn0": [("amt", 1, "am2_ready"), ("sb2", 1, "y2_ready"), ("f2", 2, "h2_ready")],
    "norm2": [("xt2", KD, "xf2_ready")],
    "proj1": [("qk1", 2 * KD, "raw_ready"), ("v1", HALF // 2, "v3_ready"), ("qr", 2 * NT, "qr_ready")],
    "score1": [("s1", 2 * NT, "ss_ready")],
    "sum1": [("pt", 2 * NT, "pt_ready"), ("pst", 2 * NT, "pst_ready"), ("pv1", NT, "a1_ready"), ("at1", KD, "af1_ready")],
    "out1": [("o1", 2, "h3_ready")],
    "norm3": [("xt3", KD, "xf3_ready")],
    "ffn1": [("fa", NT, "out_ready"), ("wt", 1, "wf_ready")],
}


def sum1_jobs(h):
    first, end = NT * h, NT * h + NT
    turned = [[(name, 2 * t + c) for name in ("pt", "pst") for c in range(KD)] for t in range(first, end)] + [[]]
    jobs = turned[0]
    for t in range(first, end):
        jobs = jobs + turned[t + 1 - first] + [("pv1", t)]
    return jobs + [("at1", KD * h + i) for i in range(KD)]


def plan_banks(banks):
    reader = {name: sem for stage in PRODUCTS.values() for name, _, sem in stage}
    jobs = []
    for stage, h in ORDER:
        if stage == "sum1":
            jobs += sum1_jobs(h)
        else:
            jobs += [(name, n * h + i) for name, n, _ in PRODUCTS[stage] for i in range(n)]
    plan, last = {}, {}
    for n, (name, i) in enumerate(jobs):
        b = n % banks
        plan[name, i] = (b, last.get(b))
        last[b] = (reader[name], i + 1)
    return plan


COLS = {}


def _columns():
    at = 0
    for name, n in [("tok_b", KD), ("qk_b", 2 * KD), ("conv_w", 3 * MH), ("conv_b", MH), ("rel_q", L), ("rel_v", E)]:
        COLS[name] = (at, n)
        at += n
    return at


NCOLS = _columns()
CONST = {}


def _constants():
    at = 0
    for name, n in [("ident", P), ("mask8", HC), ("mask3", H), ("causal", L), ("cos_q", L), ("sin_q", L),
                    ("cos_k", L), ("sin_k", L)]:
        CONST[name] = (at, n)
        at += n
    return at


NCONST = _constants()
ROWP = {"v_b": (0, D), "o_b": (D, D), "base_b": (2 * D, D), "router_b": (3 * D, EXPERTS)}
NROW = 3 * D + EXPERTS


def build(nc, x, tok_w, pos, cols, rows, const, qkv0_w, o0_w, w1, w2, qkv1_w, o1_w, ffn1_w, lora_b, out):
    ctx = ExitStack()
    with ctx:
        def sb(name, shape, dt=F32):
            return ctx.enter_context(nc.sbuf_tensor(name, shape, dt))

        sems = {}

        def sem(name):
            if name not in sems:
                sems[name] = ctx.enter_context(nc.semaphore(name))
            return sems[name]

        psum = ctx.enter_context(nc.psum_tensor("psum", [P, 8, 512], F32))
        plan = plan_banks(8)

        tok_arena = sb("tok_arena", [P, KP * B * L + KP * D])
        x_sb = tok_arena[:, 0:KP * B * L].rearrange("p (k n) -> p k n", k=KP)
        tokw_sb = tok_arena[:, KP * B * L:].rearrange("p (k n) -> p k n", k=KP)
        w_arena = sb("w_arena", [P, TILES * L * H])
        w1_sb = w_arena[:, 0:KD * HID]
        w2_sb = w_arena[:, KD * HID:KD * HID + MH * D]
        pos_sb = sb("pos_sb", [P, KD, L])
        cols_sb = sb("cols_sb", [P, NCOLS])
        rows_sb = sb("rows_sb", [P, NROW])
        const_sb = sb("const_sb", [P, NCONST])
        attn0_w = sb("attn0_w", [P, KD * 4 * D])
        qkv0_sb = attn0_w[:, 0:KD * 3 * D].rearrange("p (k n) -> p k n", k=KD)
        o0_sb = attn0_w[:, KD * 3 * D:].rearrange("p (k n) -> p k n", k=KD)
        x3 = attn0_w[:, 0:KD * HALF * G3].rearrange("p (k i r) -> p k i r", k=KD, r=G3)
        qkv1_sb = sb("qkv1_sb", [P, KD, 3 * D])
        o1_sb = sb("o1_sb", [P, KD, D])
        ffn1_sb = sb("ffn1_sb", [P, KD, FA])
        lorab_sb = sb("lorab_sb", [P, D])
        w1t = sb("w1t", [P, KD, HID], BF16)
        w2t = sb("w2t", [P, MH, D], BF16)
        ident_bf = sb("ident_bf", [P, P], BF16)
        ones = sb("ones", [P, P])
        rel_block = sb("rel_block", [P, L, HC])
        rel_value = sb("rel_value", [P, H, VW])
        qk_bias = sb("qk_bias", [P, 2 * KD])
        wabs = sb("wabs", [P, 2])
        wscale = sb("wscale", [P, 2])
        wscale_127 = sb("wscale_127", [P, 2])
        winv = sb("winv", [P, 2])

        eps_col = sb("eps_col", [P, 1])

        def col(name):
            a, n = COLS[name]
            return cols_sb[:, a:a + n]

        def row(name):
            a, n = ROWP[name]
            return rows_sb[:, a:a + n]

        def cst(name):
            a, n = CONST[name]
            return const_sb[:, a:a + n]

        ident, mask8, mask3, causal = cst("ident"), cst("mask8"), cst("mask3"), cst("causal")

        h0 = sb("h0", [P, TILES, D])
        res = sb("res", [P, TILES, D])
        xn = sb("xn", [P, TILES, D])
        xfa = sb("xfa", [P, KD, B, SLOT])
        xfb = sb("xfb", [P, KD, B, SLOT])
        stats = sb("stats", [P, TILES, 6])
        mv = sb("mv", [P, TILES, 2])
        std = sb("std", [P, TILES])
        rstd = sb("rstd", [P, TILES])
        qk_f = sb("qk_f", [P, 2, 2, KD, TOK])
        spread = sb("spread", [P, KD, HC, TOK])
        v_arena = sb("v_arena", [P, B * H * VW])
        v2 = v_arena[:, :].rearrange("p (q b i h e) -> p q b i h e", q=B // 4, b=2, i=2, h=H)
        v3 = v_arena[:, :].rearrange("p (i h e) -> p i h e", i=B, h=H)
        v_half = B * H * VW // 2
        q2 = [v_arena[:, h * v_half:h * v_half + MH * HALF * SLOT // 2].bitcast(BF16)
              .rearrange("p (m i s) -> p m i s", m=MH, s=SLOT) for h in (0, 1)]
        s_arena = sb("s_arena", [P, TILES * H * L])
        st = s_arena[:, :].rearrange("p (t h k) -> p t h k", t=TILES, h=H)
        hid = [s_arena[:, h * MH * TOK:(h + 1) * MH * TOK].rearrange("p (m n) -> p m n", m=MH) for h in (0, 1)]
        sc = s_arena[:, :].rearrange("p (t k h) -> p t k h", t=TILES, h=H)
        zs = w_arena[:, :].rearrange("p (t k h) -> p t k h", t=TILES, h=H)
        fill = s_arena[0:96, 0:2 * (L - 1) * H].rearrange("p (a x) -> p a x", a=2)
        PT = 2 * 2 * len(SEL) * ROWS
        rot = [tok_arena[:, h * 2 * PT:h * 2 * PT + 8 * TOK].rearrange("p (s a k n) -> p s a k n", s=2, a=2, k=KD) for h in (0, 1)]
        raw, swap = [r[:, 0] for r in rot], [r[:, 1] for r in rot]
        ptf, pstf = [tok_arena[:, a * PT:(a + 1) * PT].rearrange("p (t n r) -> p t n r", t=2, r=ROWS) for a in (0, 1)]
        NZ = 3
        h0_flat = h0[:, :, :].rearrange("p t d -> p (t d)")
        ph = h0_flat[:, 0:2 * H * L].rearrange("p (t n) -> p t n", t=2)
        zh = h0_flat[:, 2 * H * L:2 * H * L + NZ * HC * L].rearrange("p (c h k) -> p c h k", c=NZ, h=HC)
        wax = tok_arena[:, 2 * PT:2 * PT + NT * P].rearrange("p (n r) -> p n r", r=P)
        waxf = tok_arena[:, 2 * PT + NT * P:2 * PT + NT * P + 2 * NT * ROWS].rearrange("p (h n r) -> p h n r", h=2, r=ROWS)
        den = sb("den", [P, TILES * H])
        rden = sb("rden", [P, TILES * H])
        amax = sb("amax", [P, TILES])
        rmax = sb("rmax", [P, TILES])
        qscale = sb("qscale", [P, TILES])
        deq = sb("deq", [P, TILES])
        xq = sb("xq", [P, TILES, D], BF16)
        xqf = sb("xqf", [P, 2, KD, TOK], BF16)
        diag = sb("diag", [P, NT, ROWS])
        sbc = sb("sbc", [P, 2, TOK])
        NG = 4
        g = sb("g", [P, NG, HALF, L + 2])
        tap = sb("tap", [P, NG, TOK])
        am = sb("am", [P, B, SLOT])
        am2 = sb("am2", [P, TILES])
        qr_sb = sb("qr_sb", [P, 2, L, H])
        top = sb("top", [P, TILES, H])
        logit = sb("logit", [P, TILES, EXPERTS])
        best = sb("best", [P, TILES, 8])
        shifted = sb("shifted", [P, TILES, EXPERTS])
        expo = sb("expo", [P, TILES, EXPERTS])
        gate = sb("gate", [P, TILES, EXPERTS])
        gsum = sb("gsum", [P, TILES])

        y_dram = nc.dram_tensor("rel_scores", [B, L, ZROW], F32, kind="Internal").ap()
        z_dram = nc.dram_tensor("rel_weights", [B, L, ZROW], F32, kind="Internal").ap()

        def skewed(dram, img):
            return bass.AP(dram.tensor, img * L * ZROW + (L - 1) * H, [[ZROW - H, L], [1, L * H]])

        def tiles(h):
            return range(NT * h, NT * h + NT)

        def bank(name, i):
            return psum[:, plan[name, i][0], :]

        def wait_spread(eng, h, a, m):
            if a == 0:
                eng.wait_ge(sem("qk0_ready"), 2 * KD * h + 2 * m + 1)
                if h == 1:
                    eng.wait_ge(sem("s0_full"), NT * (m + 1))
            else:
                eng.wait_ge(sem("rope_ready"), 2 * h + 2)
                if h == 0:
                    eng.wait_ge(sem("s0_full"), 2 * NT + NT * (m + 1))
                else:
                    eng.wait_ge(sem("s1_full"), 2 * NT - KD + m + 1)

        block = ctx.enter_context(nc.Block())

        @block.sync
        def _(sp):
            def load(name, dst, src):
                sp.dma_start(dst, src).then_inc(sem(name), 16)

            load("cols_in", cols_sb[:, :], cols)
            load("const_in", const_sb[:, :], const)
            load("pos_in", pos_sb[:, :, :], pos)
            load("tokw_in", tokw_sb, tok_w)
            for h in (0, 1):
                load(f"x{h}_in", x_sb[:, :, h * TOK:(h + 1) * TOK], x[:, :, h * TOK:(h + 1) * TOK])
            load("rows_in", rows_sb[:, :], rows.to_broadcast([P, NROW]))
            load("qkv0_in", qkv0_sb, qkv0_w)
            load("w1_in", w1_sb, w1)
            load("w2_in", w2_sb, w2)
            load("o0_in", o0_sb, o0_w)
            load("qkv1_in", qkv1_sb[:, :, :], qkv1_w)
            load("o1_in", o1_sb[:, :, :], o1_w)
            load("ffn1_in", ffn1_sb[:, :, :], ffn1_w)
            load("lorab_in", lorab_sb[:, :], lora_b)
            sp.wait_ge(sem("fill_ready"), 2)
            y_rows = y_dram.rearrange("i q r -> (i q) r")
            z_rows = z_dram.rearrange("i q r -> (i q) r")
            reps = B * L // 96
            sp.dma_start(y_rows[:, L * H:].rearrange("(a p) x -> p a x", p=96),
                         fill[:, 0].unsqueeze(1).to_broadcast([96, reps, (L - 1) * H])).then_inc(sem("y_filled"), 16)
            sp.dma_start(z_rows[:, 0:(L - 1) * H].rearrange("(a p) x -> p a x", p=96),
                         fill[:, 1].unsqueeze(1).to_broadcast([96, reps, (L - 1) * H])).then_inc(sem("z_filled"), 16)

            def store_qr(t):
                sp.wait_ge(sem("qr_ready"), 2 * t + 2)
                for b in range(2):
                    sp.dma_start(y_dram[2 * t + b, :, 0:L * H], qr_sb[SLOT * b:SLOT * b + L, t % 2].rearrange("p r h -> p (r h)"))\
                      .then_inc(sem(f"qr_stored{t % 2}"), 16)

            def load_rel(t):
                if t == 0:
                    sp.wait_ge(sem("y_filled"), 16)
                sp.wait_ge(sem(f"qr_stored{t % 2}"), 32 * (t // 2 + 1))
                for b in range(2):
                    sp.dma_start(sc[SLOT * b:SLOT * b + L, t].rearrange("p k h -> p (k h)"), skewed(y_dram, 2 * t + b))\
                      .then_inc(sem(f"rel_in{t}"), 16)

            def store_p(t):
                if t == 0:
                    sp.wait_ge(sem("z_filled"), 16)
                sp.wait_ge(sem("p_ready"), t + 1)
                for b in range(2):
                    sp.dma_start(skewed(z_dram, 2 * t + b), sc[SLOT * b:SLOT * b + L, t].rearrange("p k h -> p (k h)"))\
                      .then_inc(sem(f"p_stored{t % 2}"), 16)

            def load_pskew(t):
                if t == 0:
                    sp.wait_ge(sem("zs_zeroed"), 1)
                sp.wait_ge(sem(f"p_stored{t % 2}"), 32 * (t // 2 + 1))
                if t >= NT:
                    sp.wait_ge(sem(f"pskew_in{t % NT}"), 32)
                for b in range(2):
                    sp.dma_start(zs[SLOT * b:SLOT * b + L, t].rearrange("p k h -> p (k h)"), z_dram[2 * t + b, :, 0:L * H])\
                      .then_inc(sem(f"pskew_in{t % NT}"), 16)

            out_v = out.rearrange("(t b) q d -> b q t d", b=2)
            for stage, h in ORDER:
                if stage in ("proj1", "score1"):
                    store, fetch = (store_qr, load_rel) if stage == "proj1" else (store_p, load_pskew)
                    for t in tiles(h):
                        store(t)
                        if t > NT * h:
                            fetch(t - 1)
                    fetch(NT * h + NT - 1)
                if stage == "ffn1":
                    for t in tiles(h):
                        sp.wait_ge(sem("out_ready"), t + 1)
                        for b in range(2):
                            sp.dma_start(out_v[b, :, t, :], xn[SLOT * b:SLOT * b + L, t, :]).then_inc(sem("stored"), 16)
            sp.wait_ge(sem("stored"), 16 * B)

        @block.tensor
        def _(pe):
            zeroed = [False]

            def claim(name, i):
                b, freed = plan[name, i]
                if not zeroed[0]:
                    pe.wait_ge(sem("psum_zeroed"), 1)
                    zeroed[0] = True
                if freed:
                    pe.wait_ge(sem(freed[0]), freed[1])
                return psum[:, b, :]

            def transposes(name, h, src):
                for c in range(KD):
                    ps = claim(name, KD * h + c)
                    for n, t in enumerate(tiles(h)):
                        last = pe.transpose(ps[:, n * P:n * P + ROWS], src[0:ROWS, t, c * P:(c + 1) * P],
                                            ident[0:ROWS, 0:ROWS])
                    last.then_inc(sem(name + "_full"), 1)

            def token_product(name, h, lhs, w):
                for j in range(2):
                    ps = claim(name, 2 * h + j)
                    for a in range(2):
                        t = NT * h + 2 * j + a
                        for k in range(KD):
                            last = pe.matmul(ps[0:ROWS, a * D:(a + 1) * D],
                                             lhs[:, k, 2 * t:2 * t + 2, :].rearrange("p i s -> p (i s)")[:, 0:ROWS],
                                             w[:, k, :], start=(a == 0 and k == 0), stop=(k == KD - 1),
                                             skip_group_check=True)
                    last.then_inc(sem(name + "_full"), 1)

            def imgs(f, k, h):
                return f[:, k, HALF * h:HALF * (h + 1), 0:L]

            def embed(h):
                pe.wait_ge(sem("tokw_in"), 16)
                pe.wait_ge(sem(f"x{h}_in"), 16)
                for m in range(KD):
                    ps = claim("embed", KD * h + m)
                    for k in range(KP):
                        last = pe.matmul(ps[:, 0:TOK], tokw_sb[:, k, m * P:(m + 1) * P],
                                         x_sb[:, k, h * TOK:(h + 1) * TOK], start=(k == 0), stop=(k == KP - 1))
                    last.then_inc(sem("embed_full"), 1)
                pe.wait_ge(sem("h0f_ready"), KD * (h + 1))
                for j in range(2):
                    ps = claim("h0t", 2 * h + j)
                    for a in range(2):
                        t = NT * h + 2 * j + a
                        for c in range(KD):
                            last = pe.transpose(ps[0:ROWS, a * D + c * P:a * D + (c + 1) * P],
                                                xfb[:, c, 2 * t:2 * t + 2, :].rearrange("p i s -> p (i s)")[:, 0:ROWS],
                                                ident)
                    last.then_inc(sem("h0t_full"), 1)

            def weights(h):
                pe.wait_ge(sem("ones_ready"), 1)
                pe.wait_ge(sem("wabs_ready"), 2)
                ps = claim("wsum", 0)
                pe.matmul(ps[:, 0:2], ones[:, :], wabs[:, :], start=True, stop=True).then_inc(sem("wsum_full"), 1)

            def norm0(h):
                pe.wait_ge(sem("xn0_ready"), h + 1)
                transposes("xt0", h, xn)

            def proj0(h):
                pe.wait_ge(sem("qkv0_in"), 16)
                pe.wait_ge(sem("xf0_ready"), KD * (h + 1))
                for m in range(KD):
                    for a in range(2):
                        ps = claim("qk0", 2 * KD * h + 2 * m + a)
                        for k in range(KD):
                            last = pe.matmul(ps[:, 0:TOK], qkv0_sb[:, k, a * D + m * P:a * D + (m + 1) * P],
                                             imgs(xfa, k, h), start=(k == 0), stop=(k == KD - 1))
                        last.then_inc(sem("qk0_full"), 1)
                for j in range(2):
                    quad = 2 * h + j
                    ps = claim("v0", quad)
                    for p in range(2):
                        for k in range(KD):
                            last = pe.matmul(ps[:, p * D:(p + 1) * D],
                                             xfa[:, k, 4 * quad + 2 * p:4 * quad + 2 * p + 2, :].rearrange("p i s -> p (i s)"),
                                             qkv0_sb[:, k, 2 * D:3 * D], start=(p == 0 and k == 0), stop=(k == KD - 1),
                                             skip_group_check=True)
                    last.then_inc(sem("v0_full"), 1)

            def score0(h):
                for m in range(KD):
                    pe.wait_ge(sem("spread0b_ready" if m else "spread0_ready"), h + 1)
                    for n in range(NT):
                        quad, p = 2 * h + n // 2, n % 2
                        ps = claim("s0", 2 * NT * h + NT * m + n)
                        for i in range(2):
                            img = 4 * (n // 2) + 2 * p + i
                            last = pe.matmul(ps[SLOT * i:SLOT * i + L, 0:HC * L], qk_f[:, h, 1, m, img * L:(img + 1) * L],
                                             spread[:, m, :, img * L:(img + 1) * L], start=True, stop=True)
                        last.then_inc(sem("s0_full"), 1)

            def sum0(h):
                pe.wait_ge(sem("v2_ready"), 2 * h + 2)
                pe.wait_ge(sem("st_ready"), 2 * NT * (h + 1))
                for j in range(2):
                    quad = 2 * h + j
                    for c in range(KD):
                        ps = claim("pv0", 4 * h + 2 * j + c)
                        sums = ps[:, 0:2 * HC * VW].rearrange("q (i h e) -> q i h e", i=2, h=HC)
                        for n in range(HC):
                            for p in range(2):
                                last = pe.matmul(sums[SLOT * p:SLOT * p + L, :, n, :], st[0:ROWS, 2 * quad + p, c * HC + n, :],
                                                 v2[0:ROWS, quad, p, :, c * HC + n, :], start=(n == 0), stop=True,
                                                 skip_group_check=True)
                        last.then_inc(sem("pv0_full"), 1)
                pe.wait_ge(sem("a0_ready"), 4 * (h + 1))
                transposes("at0", h, xn)

            def out0(h):
                pe.wait_ge(sem("af0_ready"), KD * (h + 1))
                pe.wait_ge(sem("o0_in"), 16)
                token_product("o0", h, xfa, o0_sb)

            def broadcast(name, h):
                ps = claim(name, h)
                for n in range(NT):
                    last = pe.matmul(ps[:, n * P:n * P + ROWS], ones[0:ROWS, :], diag[0:ROWS, n, :], start=True, stop=True,
                                     skip_group_check=True)
                last.then_inc(sem(name + "_full"), 1)

            def norm1(h):
                pe.wait_ge(sem("xq_ready"), h + 1)
                pe.wait_ge(sem("identbf_ready"), 1)
                ps = claim("xt1", h).bitcast(BF16)
                for k in range(KD):
                    for n, t in enumerate(tiles(h)):
                        last = pe.transpose(ps[:, (k * NT + n) * P:(k * NT + n) * P + ROWS], xq[0:ROWS, t, k * P:(k + 1) * P],
                                            ident_bf[0:ROWS, 0:ROWS])
                last.then_inc(sem("xt1_full"), 1)
                pe.wait_ge(sem("diag1_ready"), h + 1)
                broadcast("sb1", h)

            def conv(h):
                pe.wait_ge(sem("xqf_ready"), h + 1)
                pe.wait_ge(sem("w1t_ready"), 1)
                for m in range(MH):
                    ps = claim("f1", MH * h + m)
                    for k in range(KD):
                        last = pe.matmul(ps[:, 0:TOK], w1t[:, k, m * P:(m + 1) * P], xqf[:, h, k, :], start=(k == 0),
                                         stop=(k == KD - 1))
                    last.then_inc(sem("f1_full"), 1)

            def ffn0(h):
                pe.wait_ge(sem("am_ready"), h + 1)
                ps = claim("amt", h)
                for n, t in enumerate(tiles(h)):
                    last = pe.transpose(ps[0:ROWS, n * P:(n + 1) * P],
                                        am[:, 2 * t:2 * t + 2, :].rearrange("p i s -> p (i s)")[:, 0:ROWS], ident)
                last.then_inc(sem("amt_full"), 1)
                pe.wait_ge(sem("diag2_ready"), h + 1)
                broadcast("sb2", h)
                pe.wait_ge(sem("q2_ready"), h + 1)
                pe.wait_ge(sem("w2t_ready"), 1)
                for j in range(2):
                    ps = claim("f2", 2 * h + j)
                    for a in range(2):
                        n = 2 * j + a
                        for m in range(MH):
                            last = pe.matmul(ps[0:ROWS, a * D:(a + 1) * D],
                                             q2[h][:, m, 2 * n:2 * n + 2, :].rearrange("p i s -> p (i s)")[:, 0:ROWS],
                                             w2t[:, m, :], start=(a == 0 and m == 0), stop=(m == MH - 1),
                                             skip_group_check=True)
                    last.then_inc(sem("f2_full"), 1)

            def norm2(h):
                pe.wait_ge(sem("xn2_ready"), h + 1)
                transposes("xt2", h, xn)

            def proj1(h):
                pe.wait_ge(sem("qkv1_in"), 16)
                pe.wait_ge(sem("xf2_ready"), KD * (h + 1))
                for a in range(2):
                    for m in range(KD):
                        ps = claim("qk1", 2 * KD * h + KD * a + m)
                        for k in range(KD):
                            last = pe.matmul(ps[:, 0:TOK], qkv1_sb[:, k, a * D + m * P:a * D + (m + 1) * P],
                                             imgs(xfb, k, h), start=(k == 0), stop=(k == KD - 1))
                        last.then_inc(sem("qk1_full"), 1)
                pe.wait_ge(sem("x3_ready"), h + 1)
                for j in range(HALF // 2):
                    ps = claim("v1", HALF // 2 * h + j)
                    for a in range(2):
                        for k in range(KD):
                            last = pe.matmul(ps[0:G3, a * D:(a + 1) * D], x3[:, k, 2 * j + a, :],
                                             qkv1_sb[:, k, 2 * D:3 * D], start=(a == 0 and k == 0), stop=(k == KD - 1),
                                             skip_group_check=True)
                    last.then_inc(sem("v1_full"), 1)
                pe.wait_ge(sem("relblock_ready"), 1)
                pe.wait_ge(sem("rope_ready"), 2 * h + 1)
                for n, t in enumerate(tiles(h)):
                    for c in range(KD):
                        ps = claim("qr", 2 * t + c)
                        for b in range(2):
                            i = 2 * n + b
                            last = pe.matmul(ps[SLOT * b:SLOT * b + L, 0:L * HC], qk_f[:, h, 0, c, i * L:(i + 1) * L],
                                             rel_block[:, :, :], start=True, stop=True)
                        last.then_inc(sem("qr_full"), 1)

            def score1(h):
                for n, t in enumerate(tiles(h)):
                    for c in range(KD):
                        if n == 0:
                            pe.wait_ge(sem("spread1b_ready" if c else "spread1_ready"), h + 1)
                        ps = claim("s1", 2 * t + c)
                        for b in range(2):
                            i = 2 * n + b
                            last = pe.matmul(ps[SLOT * b:SLOT * b + L, 0:HC * L], qk_f[:, h, 0, c, i * L:(i + 1) * L],
                                             spread[:, c, :, i * L:(i + 1) * L], start=True, stop=True)
                        last.then_inc(sem("s1_full"), 1)

            def sum1(h):
                def turn(t):
                    for name in ("pt", "pst"):
                        if name == "pt":
                            pe.wait_ge(sem("ph_ready"), t + 1)
                        for c in range(KD):
                            if name == "pst":
                                pe.wait_ge(sem("zh_ready"), 2 * t + c + 1)
                                src = zh[0:ROWS, (2 * t + c) % NZ].rearrange("p h k -> p (h k)")
                            else:
                                src = ph[0:ROWS, t % 2, c * HC * L:(c + 1) * HC * L]
                            ps = claim(name, 2 * t + c)
                            for n3, (a, z) in enumerate(SEL):
                                last = pe.transpose(ps[0:(z - a) * L, n3 * P:n3 * P + ROWS], src[:, a * L:z * L],
                                                    ident[0:ROWS, 0:ROWS])
                            last.then_inc(sem(name + "_full"), 1)

                turn(NT * h)
                for n, t in enumerate(tiles(h)):
                    if t + 1 < NT * (h + 1):
                        turn(t + 1)
                    if n == 0:
                        pe.wait_ge(sem("relvalue_ready"), 1)
                        pe.wait_ge(sem("v3_ready"), HALF // 2 * (h + 1))
                        pe.wait_ge(sem("v3_ones"), h + 1)
                    ps = claim("pv1", t)
                    pe.wait_ge(sem("pst_ready"), 2 * t + 2)
                    for c in range(KD):
                        for n3, (a, z) in enumerate(SEL):
                            k, w = (z - a) * L, slice((c * HC + a) * VW, (c * HC + z) * VW)
                            pe.matmul(ps[0:ROWS, w], pstf[0:k, t % 2, 3 * c + n3, :],
                                      rel_value[0:k, c * HC + a:c * HC + z, :], start=(c == 0 and n3 == 0), stop=False,
                                      skip_group_check=True)
                    pe.wait_ge(sem("pt_ready"), 2 * t + 2)
                    for c in range(KD):
                        for n3, (a, z) in enumerate(SEL):
                            k, w = (z - a) * L, slice((c * HC + a) * VW, (c * HC + z) * VW)
                            for b in range(2):
                                last = pe.matmul(ps[SLOT * b:SLOT * b + L, w], ptf[0:k, t % 2, 3 * c + n3, SLOT * b:SLOT * b + L],
                                                 v3[0:k, 2 * t + b, c * HC + a:c * HC + z, :], start=False, stop=True,
                                                 skip_group_check=True)
                    last.then_inc(sem("pv1_full"), 1)
                pe.wait_ge(sem("a1_ready"), NT * (h + 1))
                transposes("at1", h, xn)

            def out1(h):
                pe.wait_ge(sem("af1_ready"), KD * (h + 1))
                pe.wait_ge(sem("o1_in"), 16)
                token_product("o1", h, xfa, o1_sb)

            def norm3(h):
                pe.wait_ge(sem("xn3_ready"), h + 1)
                transposes("xt3", h, xn)

            def ffn1(h):
                pe.wait_ge(sem("ffn1_in"), 16)
                pe.wait_ge(sem("xf3_ready"), KD * (h + 1))
                for t in tiles(h):
                    ps = claim("fa", t)
                    for k in range(KD):
                        last = pe.matmul(ps[0:ROWS, 0:FA], xfb[:, k, 2 * t:2 * t + 2, :].rearrange("p i s -> p (i s)")[:, 0:ROWS],
                                         ffn1_sb[:, k, :], start=(k == 0), stop=(k == KD - 1), skip_group_check=True)
                    last.then_inc(sem("fa_full"), 1)
                pe.wait_ge(sem("wax_ready"), h + 1)
                ps = claim("wt", h)
                for n in range(NT):
                    last = pe.transpose(ps[:, n * P:n * P + ROWS], wax[0:ROWS, n, :], ident[0:ROWS, 0:ROWS])
                last.then_inc(sem("wt_full"), 1)
                pe.wait_ge(sem("wf_ready"), h + 1)
                pe.wait_ge(sem("lorab_in"), 16)
                for n, t in enumerate(tiles(h)):
                    pe.matmul(bank("fa", t)[0:ROWS, 0:D], waxf[:, h, n, :], lorab_sb[:, :], start=False, stop=True,
                              skip_group_check=True).then_inc(sem("fb_full"), 1)

            pe.wait_ge(sem("const_in"), 16)
            pe_stages = {"embed": embed, "norm0": norm0, "weights": weights, "proj0": proj0, "score0": score0, "sum0": sum0, "out0": out0,
                          "norm1": norm1, "conv": conv, "ffn0": ffn0, "norm2": norm2, "proj1": proj1, "score1": score1, "sum1": sum1,
                          "out1": out1, "norm3": norm3, "ffn1": ffn1}
            pe.wait_ge(sem("xfb_zeroed"), 1)
            for stage, h in ORDER:
                if stage in pe_stages:
                    pe_stages[stage](h)

        @block.scalar
        def _(act):
            def weights(h):
                act.wait_ge(sem("w1_in"), 16)
                nc.scalar.activation(w1t[:, :, :].rearrange("p k n -> p (k n)"), w1_sb, ACT.Abs, accum_out=wabs[:, 0:1])\
                  .then_inc(sem("wabs_ready"), 1)
                act.wait_ge(sem("w2_in"), 16)
                nc.scalar.activation(w2t[:, :, :].rearrange("p k n -> p (k n)"), w2_sb, ACT.Abs, accum_out=wabs[:, 1:2])\
                  .then_inc(sem("wabs_ready"), 1)

            def root(s, h):
                act.wait_ge(sem("mv_ready"), LN_AT[s, h])
                t = slice(NT * h, NT * h + NT)
                nc.scalar.activation(std[0:ROWS, t], mv[0:ROWS, t, 1], ACT.Sqrt, bias=eps_col[0:ROWS, :])\
                  .then_inc(sem("std_ready"), 1)

            def to_features(name, ready, h, dst):
                for c in range(KD):
                    act.wait_ge(sem(name + "_full"), KD * h + c + 1)
                    nc.scalar.copy(dst[:, c, HALF * h:HALF * (h + 1), 0:L],
                                   bank(name, KD * h + c).rearrange("p (i s) -> p i s", s=SLOT)[:, :, 0:L])\
                      .then_inc(sem(ready), 1)

            def embed(h):
                for j in range(2):
                    act.wait_ge(sem("h0t_full"), 2 * h + j + 1)
                    t = NT * h + 2 * j
                    nc.scalar.copy(h0[0:ROWS, t:t + 2, :].rearrange("p t d -> p (t d)"), bank("h0t", 2 * h + j)[0:ROWS, :])\
                      .then_inc(sem("h0_ready"), 1)

            def norm0(h):
                root(0, h)
                if h == 0:
                    act.wait_ge(sem("xfa_zeroed"), 1)
                for c in range(KD):
                    act.wait_ge(sem("xt0_full"), KD * h + c + 1)
                    for q in range(HALF // 4):
                        a = HALF * h + 4 * q
                        last = nc.scalar.copy(xfa[:, c, a:a + 4, 0:L].rearrange("f (p i) s -> f i p s", i=2),
                                              bank("xt0", KD * h + c)[:, 4 * SLOT * q:4 * SLOT * (q + 1)]
                                              .rearrange("f (i p s) -> f i p s", i=2, s=SLOT)[:, :, :, 0:L])
                    last.then_inc(sem("xf0_ready"), 1)

            def spread0(h):
                wait_spread(act, h, 0, 1)
                for n in range(HC):
                    last = nc.scalar.activation(spread[:, 1, n, :], qk_f[:, h, 0, 1, :], ACT.Copy, scale=mask8[:, n:n + 1])
                last.then_inc(sem("spread0b_ready"), 1)

            def score0(h):
                if h == 0:
                    act.wait_ge(sem("const_in"), 16)
                spread0(h)

            def sum0(h):
                to_features("at0", "af0_ready", h, xfa)

            def norm1(h):
                root(1, h)
                act.wait_ge(sem("xt1_full"), h + 1)
                nc.scalar.copy(xqf[:, h, :, :].rearrange("p k (i q) -> p (k i) q", q=L),
                               bank("xt1", h).bitcast(BF16).rearrange("p (i s) -> p i s", s=SLOT)[:, :, 0:L])\
                  .then_inc(sem("xqf_ready"), 1)
                act.wait_ge(sem("sb1_full"), h + 1)
                nc.scalar.copy(sbc[:, h, :].rearrange("p (i q) -> p i q", q=L),
                               bank("sb1", h).rearrange("p (i s) -> p i s", s=SLOT)[:, :, 0:L]).then_inc(sem("sb1_ready"), 1)

            def conv(h):

                def silu(i):
                    act.wait_ge(sem("conv_ready"), i + 1)
                    m = i % MH
                    nc.scalar.activation(hid[h][:, m, :], tap[:, i % NG, :], ACT.Silu).then_inc(sem("hid_ready"), 1)

                for m in range(MH):
                    i = MH * h + m
                    act.wait_ge(sem("g_ready"), i + 1)
                    cw, cb = col("conv_w"), col("conv_b")
                    if i >= NG:
                        act.wait_ge(sem("hid_ready"), i - NG + 1)
                    nc.scalar.activation(tap[:, i % NG, :].rearrange("p (i q) -> p i q", q=L), g[:, i % NG, :, 0:L],
                                         ACT.Identity, scale=cw[:, 3 * m:3 * m + 1], bias=cb[:, m:m + 1])\
                      .then_inc(sem("tap_ready"), 1)
                    if m >= 2:
                        silu(i - 2)
                silu(MH * h + MH - 2)
                silu(MH * h + MH - 1)

            def norm2(h):
                root(2, h)
                to_features("xt2", "xf2_ready", h, xfb)

            def proj1(h):
                for n in range(2 * KD):
                    act.wait_ge(sem("qk1_full"), 2 * KD * h + n + 1)
                    nc.scalar.copy(raw[h][:, n // KD, n % KD, :], bank("qk1", 2 * KD * h + n)[:, 0:TOK])\
                      .then_inc(sem("raw_ready"), 1)
                for t in tiles(h):
                    if t >= 2:
                        act.wait_ge(sem(f"qr_stored{t % 2}"), 32 * (t // 2))
                    for c in range(KD):
                        act.wait_ge(sem("qr_full"), 2 * t + c + 1)
                        nc.scalar.copy(qr_sb[0:ROWS, t % 2, :, c * HC:(c + 1) * HC],
                                       bank("qr", 2 * t + c)[0:ROWS, 0:L * HC].rearrange("p (r h) -> p r h", h=HC))\
                          .then_inc(sem("qr_ready"), 1)

            def spread1(h):
                wait_spread(act, h, 1, 1)
                for n in range(HC):
                    last = nc.scalar.activation(spread[:, 1, n, :], qk_f[:, h, 1, 1, :], ACT.Copy, scale=mask8[:, n:n + 1])
                last.then_inc(sem("spread1b_ready"), 1)

            def score1(h):
                spread1(h)
                for t in tiles(h):
                    act.wait_ge(sem("shift_ready"), t + 1)
                    flat = sc[0:ROWS, t].rearrange("p k h -> p (k h)")
                    nc.scalar.activation(flat, flat, ACT.Exp).then_inc(sem("p_ready"), 1)

            def sum1(h):
                for t in tiles(h):
                    for name, dst in (("pt", ptf), ("pst", pstf)):
                        for c in range(KD):
                            act.wait_ge(sem(name + "_full"), 2 * t + c + 1)
                            if t >= 2 and c == 0:
                                act.wait_ge(sem("pv1_full"), t - 1)
                            nc.scalar.copy(dst[0:G3, t % 2, 3 * c:3 * c + 3, :],
                                           bank(name, 2 * t + c).rearrange("p (n s) -> p n s", s=P)[0:G3, 0:3, 0:ROWS])\
                              .then_inc(sem(name + "_ready"), 1)

                to_features("at1", "af1_ready", h, xfa)

            def norm3(h):
                root(3, h)
                to_features("xt3", "xf3_ready", h, xfb)

            def ffn1(h):
                act.wait_ge(sem("lshift_ready"), h + 1)
                t = slice(NT * h, NT * h + NT)
                nc.scalar.activation(expo[0:ROWS, t, :], shifted[0:ROWS, t, :], ACT.Exp).then_inc(sem("expo_ready"), 1)
                act.wait_ge(sem("wt_full"), h + 1)
                nc.scalar.copy(waxf[:, h, :, :], bank("wt", h).rearrange("p (n s) -> p n s", s=P)[:, :, 0:ROWS])\
                  .then_inc(sem("wf_ready"), 1)

            act.wait_ge(sem("eps_ready"), 1)
            act_stages = {"embed": embed, "norm0": norm0, "weights": weights, "score0": score0, "sum0": sum0, "norm1": norm1, "conv": conv, "norm2": norm2,
                          "proj1": proj1, "score1": score1, "sum1": sum1, "norm3": norm3, "ffn1": ffn1}
            for stage, h in ORDER:
                if stage in act_stages:
                    act_stages[stage](h)

        @block.gpsimd
        def _(pool):
            steps = [0]

            def link(ins):
                steps[0] += 1
                ins.then_inc(sem("pool_step"), 1)
                pool.wait_ge(sem("pool_step"), steps[0])

            pool.memset(xfb[:, :, :, :], 0.0).then_inc(sem("xfb_zeroed"), 1)
            pool.memset(ones[:, :], 1.0).then_inc(sem("ones_ready"), 1)
            pool.memset(xfa[:, :, :, :], 0.0).then_inc(sem("xfa_zeroed"), 1)
            pool.memset(fill[:, 0], NEG).then_inc(sem("fill_ready"), 1)
            pool.memset(fill[:, 1], 0.0).then_inc(sem("fill_ready"), 1)
            pool.memset(v_arena[:, :], 0.0).then_inc(sem("v2_zeroed"), 1)
            pool.wait_ge(sem("v2_zeroed"), 1)
            for i in range(2):
                pool.memset(v2[SLOT * i:SLOT * i + L, :, :, i, :, E].rearrange("p q b h -> p (q b) h"), 1.0)\
                    .then_inc(sem("v2_ones"), 1)
                pool.wait_ge(sem("v2_ones"), i + 1)
            pool.memset(g[:, :, :, :].rearrange("p n i q -> p (n i q)"), 0.0).then_inc(sem("g_zeroed"), 1)
            pool.memset(am[:, :, :], 0.0).then_inc(sem("am_zeroed"), 1)
            pool.wait_ge(sem("const_in"), 16)
            pool.wait_ge(sem("cols_in"), 16)
            pool.tensor_copy(ident_bf[:, :], ident).then_inc(sem("identbf_ready"), 1)
            pool.tensor_tensor(rel_block[:, :, :], col("rel_q").unsqueeze(2).to_broadcast([P, L, HC]),
                               mask8.unsqueeze(1).to_broadcast([P, L, HC]), ALU.mult).then_inc(sem("relblock_ready"), 1)
            link(pool.memset(rel_value[:, :, :], 0.0))
            pool.tensor_tensor(rel_value[:, :, 0:E], col("rel_v").unsqueeze(1).to_broadcast([P, H, E]),
                               mask3.unsqueeze(2).to_broadcast([P, H, E]), ALU.mult).then_inc(sem("relvalue_ready"), 1)

            def ternary(n, w, wt, ready):
                link(pool.tensor_scalar(w, w, winv[:, n:n + 1], ROUND, ALU.mult, ALU.add))
                link(pool.tensor_scalar(w, w, ROUND, 1.0, ALU.subtract, ALU.min))
                pool.tensor_scalar(wt, w, -1.0, None, ALU.max).then_inc(sem(ready), 1)

            def embed(h):
                t = slice(NT * h, NT * h + NT)
                if h == 0:
                    pool.wait_ge(sem("rows_in"), 16)
                pool.wait_ge(sem("h0_ready"), 2 * (h + 1))
                pool.tensor_tensor(res[0:ROWS, t, :], h0[0:ROWS, t, :],
                                   row("o_b")[0:ROWS].unsqueeze(1).to_broadcast([ROWS, NT, D]), ALU.add)\
                    .then_inc(sem("res_ready"), 1)

            def weights(h):
                pool.wait_ge(sem("wscale_ready"), 1)
                ternary(0, w1_sb, w1t[:, :, :].rearrange("p k n -> p (k n)"), "w1t_ready")
                ternary(1, w2_sb, w2t[:, :, :].rearrange("p k n -> p (k n)"), "w2t_ready")

            def sum0(h):
                pool.wait_ge(sem("pv0_full"), 4 * (h + 1))
                pool.memset(v_arena[:, h * v_half:h * v_half + MH * HALF * SLOT // 2], 0.0).then_inc(sem("q2_zeroed"), 1)

            def proj1(h):
                if h == 0:
                    pool.wait_ge(sem("w1t_ready"), 1)
                    pool.wait_ge(sem("w2t_ready"), 1)
                    pool.memset(zs[:, :, :, :].rearrange("p t k h -> p (t k h)"), 0.0).then_inc(sem("zs_zeroed"), 1)
                pool.wait_ge(sem("xf2_ready"), KD * (h + 1))
                if h == 0:
                    pool.wait_ge(sem("o0_full"), 4)
                else:
                    pool.wait_ge(sem("v1_full"), HALF // 2)
                for k in range(KD):
                    last = pool.tensor_copy(x3[:, k].rearrange("p i (a s) -> p i a s", a=3),
                                            xfb[:, k, HALF * h:HALF * (h + 1), 0:L].unsqueeze(2).to_broadcast([P, HALF, 3, L]))
                last.then_inc(sem("x3_ready"), 1)
                pool.wait_ge(sem("f2_full"), 2 * (h + 1))
                pool.tensor_copy(v3[0:G3, HALF * h:HALF * (h + 1), :, E], mask3[0:G3].unsqueeze(1).to_broadcast([G3, HALF, H]))\
                    .then_inc(sem("v3_ones"), 1)
                for a in range(2):
                    c, s = ("cos_q", "sin_q") if a == 0 else ("cos_k", "sin_k")
                    pool.wait_ge(sem("swap_ready"), 2 * h + a + 1)
                    r = raw[h][:, a].rearrange("p k (i q) -> p (k i) q", q=L)
                    w = swap[h][:, a].rearrange("p k (i q) -> p (k i) q", q=L)
                    link(pool.tensor_tensor(r, r, cst(c).unsqueeze(1).to_broadcast([P, KD * HALF, L]), ALU.mult))
                    pool.wait_ge(sem("sin_ready"), 2 * h + a + 1)
                    pool.tensor_tensor(qk_f[:, h, a].rearrange("p k n -> p (k n)"), r.rearrange("p i q -> p (i q)"),
                                       w.rearrange("p i q -> p (i q)"), ALU.add).then_inc(sem("rope_ready"), 1)

            def score1(h):
                for t in tiles(h):
                    pool.wait_ge(sem("top_ready"), t + 1)
                    pool.tensor_tensor(sc[0:ROWS, t], sc[0:ROWS, t], top[0:ROWS, t, :].unsqueeze(1).to_broadcast([ROWS, L, H]),
                                       ALU.subtract).then_inc(sem("shift_ready"), 1)

            def sum1(h):
                for t in tiles(h):
                    pool.wait_ge(sem(f"pskew_in{t % NT}"), 32 * (t // NT + 1))
                    for c in range(KD):
                        i = KD * t + c
                        if i >= NZ:
                            pool.wait_ge(sem("pst_full"), i - NZ + 1)
                        pool.tensor_copy(zh[0:ROWS, i % NZ], zs[0:ROWS, t, :, c * HC:(c + 1) * HC].rearrange("p k h -> p h k"))\
                            .then_inc(sem("zh_ready"), 1)

            def norm3(h):
                t = slice(NT * h, NT * h + NT)
                pool.wait_ge(sem("h3_ready"), 2 * (h + 1))
                pool.wait_ge(sem("xn3_ready"), h + 1)
                pool.tensor_tensor(res[0:ROWS, t, :], res[0:ROWS, t, :],
                                   row("base_b")[0:ROWS].unsqueeze(1).to_broadcast([ROWS, NT, D]), ALU.add)\
                    .then_inc(sem("res_final"), 1)

            pool_stages = {"embed": embed, "weights": weights, "sum0": sum0, "proj1": proj1, "score1": score1, "sum1": sum1,
                           "norm3": norm3}
            for stage, h in ORDER:
                if stage in pool_stages:
                    pool_stages[stage](h)

        @block.vector
        def _(dve):
            steps = [0]

            def link(ins):
                steps[0] += 1
                ins.then_inc(sem("dve_step"), 1)
                dve.wait_ge(sem("dve_step"), steps[0])

            dve.memset(eps_col[:, :], LN_EPS).then_inc(sem("eps_ready"), 1)
            dve.memset(psum[:, :, :].rearrange("p b n -> p (b n)"), 0.0).then_inc(sem("psum_zeroed"), 1)
            dve.wait_ge(sem("cols_in"), 16)
            dve.tensor_scalar(qk_bias[:, :], col("qk_b"), FEATURE_EPS, None, ALU.add).then_inc(sem("qkbias_ready"), 1)

            def norm(s, h):
                src = h0 if s == 0 else res
                for t in tiles(h):
                    last = dve.bn_stats(stats[0:ROWS, t, :], src[0:ROWS, t, :])
                link(last)
                for t in tiles(h):
                    last = dve.bn_aggr(mv[0:ROWS, t, :], stats[0:ROWS, t, :])
                last.then_inc(sem("mv_ready"), 1)
                ts = slice(NT * h, NT * h + NT)
                dve.wait_ge(sem("std_ready"), LN_AT[s, h])
                link(dve.reciprocal(rstd[0:ROWS, ts], std[0:ROWS, ts]))
                for t in tiles(h):
                    last = dve.tensor_scalar(xn[0:ROWS, t, :], src[0:ROWS, t, :], mv[0:ROWS, t, 0:1], rstd[0:ROWS, t:t + 1],
                                             ALU.subtract, ALU.mult)
                last.then_inc(sem(f"xn{s}_ready"), 1)

            def add_residual(name, ready, h):
                for j in range(2):
                    dve.wait_ge(sem(name + "_full"), 2 * h + j + 1)
                    t = NT * h + 2 * j
                    r = res[0:ROWS, t:t + 2, :].rearrange("p t d -> p (t d)")
                    dve.tensor_tensor(r, bank(name, 2 * h + j)[0:ROWS, :], r, ALU.add).then_inc(sem(ready), 1)

            def divide(sums, at, dst, ready):
                d = den[0:ROWS, at:at + H].rearrange("p (a h) -> p a h", h=sums.shape[2])
                r = rden[0:ROWS, at:at + H].rearrange("p (a h) -> p a h", h=sums.shape[2])
                link(dve.tensor_scalar(d, sums[:, :, :, E], DEN_EPS, None, ALU.max))
                link(dve.reciprocal(r, d))
                a, n = sums.shape[1], sums.shape[2]
                dve.tensor_tensor(dst, sums[:, :, :, 0:E], r.unsqueeze(3).to_broadcast([ROWS, a, n, E]), ALU.mult)\
                    .then_inc(sem(ready), 1)

            def embed(h):
                if h == 0:
                    dve.wait_ge(sem("xfb_zeroed"), 1)
                    dve.wait_ge(sem("pos_in"), 16)
                for m in range(KD):
                    dve.wait_ge(sem("embed_full"), KD * h + m + 1)
                    dve.scalar_tensor_tensor(out=xfb[:, m, HALF * h:HALF * (h + 1), 0:L],
                                             in0=bank("embed", KD * h + m)[:, 0:TOK].rearrange("p (i q) -> p i q", q=L),
                                             scalar=col("tok_b")[:, m:m + 1],
                                             in1=pos_sb[:, m, :].unsqueeze(1).to_broadcast([P, HALF, L]),
                                             op0=ALU.add, op1=ALU.add).then_inc(sem("h0f_ready"), 1)

            def norm0(h):
                dve.wait_ge(sem("h0_ready"), 2 * (h + 1))
                norm(0, h)

            def proj0(h):
                if h == 0:
                    dve.wait_ge(sem("qkbias_ready"), 1)
                    dve.wait_ge(sem("const_in"), 16)
                for m in range(KD):
                    for a in range(2):
                        n = 2 * KD * h + 2 * m + a
                        dve.wait_ge(sem("qk0_full"), n + 1)
                        dve.tensor_scalar(qk_f[:, h, a, m, :], bank("qk0", n)[:, 0:TOK], qk_bias[:, KD * a + m:KD * a + m + 1],
                                          FEATURE_EPS, ALU.add, ALU.max).then_inc(sem("qk0_ready"), 1)
                if h == 0:
                    dve.wait_ge(sem("v2_ones"), 2)
                    dve.wait_ge(sem("rows_in"), 16)
                for j in range(2):
                    quad = 2 * h + j
                    dve.wait_ge(sem("v0_full"), quad + 1)
                    vals = bank("v0", quad).rearrange("p (b h e) -> p b h e", b=2, h=H)
                    for i in range(2):
                        r = slice(SLOT * i, SLOT * i + L)
                        bias = row("v_b")[r].rearrange("p (h e) -> p h e", h=H)
                        for p in range(2):
                            last = dve.tensor_tensor(v2[r, quad, p, i, :, 0:E], vals[r, p], bias, ALU.add)
                    last.then_inc(sem("v2_ready"), 1)

            def spread0(h):
                wait_spread(dve, h, 0, 0)
                for n in range(HC):
                    last = dve.tensor_scalar(spread[:, 0, n, :], qk_f[:, h, 0, 0, :], mask8[:, n:n + 1], None, ALU.mult)
                last.then_inc(sem("spread0_ready"), 1)

            def score0(h):
                spread0(h)
                if h == 0:
                    dve.wait_ge(sem("y_filled"), 16)
                    dve.wait_ge(sem("z_filled"), 16)
                for m in range(KD):
                    for n in range(NT):
                        i = 2 * NT * h + NT * m + n
                        dve.wait_ge(sem("s0_full"), i + 1)
                        dve.tensor_tensor(st[0:ROWS, NT * h + n, m * HC:(m + 1) * HC, :],
                                          bank("s0", i)[0:ROWS, 0:HC * L].rearrange("p (h q) -> p h q", h=HC),
                                          causal[0:ROWS].unsqueeze(1).to_broadcast([ROWS, HC, L]), ALU.mult)\
                            .then_inc(sem("st_ready"), 1)

            def sum0(h):
                for j in range(2):
                    for c in range(KD):
                        i = 4 * h + 2 * j + c
                        dve.wait_ge(sem("pv0_full"), i + 1)
                        sums = bank("pv0", i)[0:ROWS, 0:2 * HC * VW].rearrange("p (i h e) -> p i h e", i=2, h=HC)
                        t = NT * h + 2 * j
                        dst = xn[0:ROWS, t:t + 2, c * P:(c + 1) * P].rearrange("p t (h e) -> p t h e", h=HC)
                        divide(sums, i * H, dst, "a0_ready")

            def out0(h):
                dve.wait_ge(sem("res_ready"), h + 1)
                add_residual("o0", "h1_ready", h)

            def diagonals(ready, h, scale):
                for n, t in enumerate(tiles(h)):
                    last = dve.tensor_scalar(diag[0:ROWS, n, :], ident[0:ROWS, 0:ROWS], scale[0:ROWS, t:t + 1], None, ALU.mult)
                last.then_inc(sem(ready), 1)

            def norm1(h):
                dve.wait_ge(sem("h1_ready"), 2 * (h + 1))
                norm(1, h)
                ts = slice(NT * h, NT * h + NT)
                dve.wait_ge(sem("xn1_ready"), h + 1)
                link(dve.tensor_reduce(amax[0:ROWS, ts], xn[0:ROWS, ts, :], AX.X, ALU.max, apply_absolute_value=True))
                link(dve.tensor_scalar(amax[0:ROWS, ts], amax[0:ROWS, ts], QUANT_EPS, None, ALU.max))
                dve.wait_ge(sem("wscale_ready"), 1)
                dve.tensor_scalar(deq[0:ROWS, ts], amax[0:ROWS, ts], wscale_127[0:ROWS, 0:1], None, ALU.mult)
                link(dve.reciprocal(rmax[0:ROWS, ts], amax[0:ROWS, ts]))
                if h == 1:
                    dve.wait_ge(sem("sb1_full"), 1)
                diagonals("diag1_ready", h, deq)
                link(dve.tensor_scalar(qscale[0:ROWS, ts], rmax[0:ROWS, ts], QMAX, None, ALU.mult))
                for t in tiles(h):
                    last = dve.tensor_scalar(xn[0:ROWS, t, :], xn[0:ROWS, t, :], qscale[0:ROWS, t:t + 1], ROUND, ALU.mult,
                                             ALU.add)
                link(last)
                dve.tensor_scalar(xq[0:ROWS, ts, :], xn[0:ROWS, ts, :], ROUND, QMAX, ALU.subtract, ALU.min)\
                    .then_inc(sem("xq_ready"), 1)

            def conv(h):
                dve.wait_ge(sem("sb1_ready"), h + 1)
                if h == 0:
                    dve.wait_ge(sem("g_zeroed"), 1)

                def add_tap(i, n, ready):
                    m = i % MH
                    t = tap[:, i % NG, :].rearrange("p (i q) -> p i q", q=L)
                    dve.scalar_tensor_tensor(out=t, in0=g[:, i % NG, :, n:L + n], scalar=col("conv_w")[:, 3 * m + n:3 * m + n + 1],
                                             in1=t, op0=ALU.mult, op1=ALU.add).then_inc(sem(ready), 1)

                for m in range(MH + 2):
                    i = MH * h + m
                    if m < MH:
                        dve.wait_ge(sem("f1_full"), i + 1)
                        if i >= NG:
                            dve.wait_ge(sem("tap_ready"), i - NG + 1)
                            dve.wait_ge(sem("conv_ready"), i - NG + 1)
                        dve.tensor_tensor(g[:, i % NG, :, 1:L + 1], bank("f1", i)[:, 0:TOK].rearrange("p (i q) -> p i q", q=L),
                                          sbc[:, h, :].rearrange("p (i q) -> p i q", q=L), ALU.mult)\
                            .then_inc(sem("g_ready"), 1)
                    if m >= 2:
                        dve.wait_ge(sem("mid_ready"), i - 1)
                        add_tap(i - 2, 2, "conv_ready")
                    if 1 <= m < MH + 1:
                        dve.wait_ge(sem("g_ready"), i)
                        dve.wait_ge(sem("tap_ready"), i)
                        add_tap(i - 1, 1, "mid_ready")
                if h == 0:
                    dve.wait_ge(sem("am_zeroed"), 1)
                dve.wait_ge(sem("hid_ready"), MH * (h + 1))
                dve.tensor_reduce(am[:, HALF * h:HALF * (h + 1), 0:L],
                                  hid[h].rearrange("p m (i q) -> p i q m", q=L), AX.X, ALU.max, apply_absolute_value=True)\
                    .then_inc(sem("am_ready"), 1)

            def ffn0(h):
                ts = slice(NT * h, NT * h + NT)
                dve.wait_ge(sem("amt_full"), h + 1)
                dve.tensor_reduce(am2[0:ROWS, ts], bank("amt", h)[0:ROWS, :].rearrange("p (t n) -> p t n", n=P), AX.X, ALU.max)\
                    .then_inc(sem("am2_ready"), 1)
                dve.wait_ge(sem("am2_ready"), h + 1)
                link(dve.tensor_scalar(am2[0:ROWS, ts], am2[0:ROWS, ts], QUANT_EPS, None, ALU.max))
                link(dve.reciprocal(rmax[0:ROWS, ts], am2[0:ROWS, ts]))
                link(dve.tensor_scalar(qscale[0:ROWS, ts], rmax[0:ROWS, ts], QMAX, None, ALU.mult))
                if h == 0:
                    dve.wait_ge(sem("sb1_full"), 2)
                else:
                    dve.wait_ge(sem("sb2_full"), 1)
                diagonals("diag2_ready", h, qscale)
                dve.tensor_scalar(deq[0:ROWS, ts], am2[0:ROWS, ts], wscale_127[0:ROWS, 1:2], None, ALU.mult)\
                    .then_inc(sem("deq2_ready"), 1)
                dve.wait_ge(sem("sb2_full"), h + 1)
                scale = bank("sb2", h).rearrange("p (i s) -> p i s", s=SLOT)[:, :, 0:L]
                hid_v = hid[h].rearrange("p m (i q) -> p m i q", q=L)
                dve.tensor_tensor(hid_v, hid_v, scale.unsqueeze(1).to_broadcast([P, MH, HALF, L]), ALU.mult)\
                    .then_inc(sem("y2_ready"), 1)
                dve.wait_ge(sem("y2_ready"), h + 1)
                dve.wait_ge(sem("q2_zeroed"), h + 1)
                dve.tensor_scalar(q2[h][:, :, :, 0:L], hid_v, ROUND, ROUND, ALU.add, ALU.subtract).then_inc(sem("q2_ready"), 1)
                dve.wait_ge(sem("deq2_ready"), h + 1)
                for j in range(2):
                    dve.wait_ge(sem("f2_full"), 2 * h + j + 1)
                    for a in range(2):
                        t = NT * h + 2 * j + a
                        last = dve.scalar_tensor_tensor(out=res[0:ROWS, t, :], in0=bank("f2", 2 * h + j)[0:ROWS, a * D:(a + 1) * D],
                                                        scalar=deq[0:ROWS, t:t + 1], in1=res[0:ROWS, t, :], op0=ALU.mult,
                                                        op1=ALU.add)
                    last.then_inc(sem("h2_ready"), 1)

            def norm2(h):
                dve.wait_ge(sem("h2_ready"), 2 * (h + 1))
                norm(2, h)

            def proj1(h):
                for a in range(2):
                    dve.wait_ge(sem("raw_ready"), 2 * KD * h + KD * (a + 1))
                    dve.stream_shuffle(swap[h][:, a].rearrange("p k n -> p (k n)"), raw[h][:, a].rearrange("p k n -> p (k n)"),
                                       mask=[p ^ 1 for p in range(32)]).then_inc(sem("swap_ready"), 1)
                    dve.wait_ge(sem("swap_ready"), 2 * h + a + 1)
                    w = swap[h][:, a].rearrange("p k (i q) -> p (k i) q", q=L)
                    dve.tensor_tensor(w, w, cst("sin_k" if a else "sin_q").unsqueeze(1).to_broadcast([P, KD * HALF, L]), ALU.mult)\
                        .then_inc(sem("sin_ready"), 1)
                dve.wait_ge(sem("f2_full"), 2 * (h + 1))
                m3 = mask3[0:G3].unsqueeze(2).to_broadcast([G3, H, E])
                for j in range(HALF // 2):
                    n = HALF // 2 * h + j
                    dve.wait_ge(sem("v1_full"), n + 1)
                    vals = bank("v1", n)[0:G3].rearrange("p (i h e) -> p i h e", i=2, h=H)
                    for a in range(2):
                        last = dve.tensor_tensor(v3[0:G3, HALF * h + 2 * j + a, :, 0:E], vals[:, a], m3, ALU.mult)
                    last.then_inc(sem("v3_ready"), 1)

            def spread1(h):
                wait_spread(dve, h, 1, 0)
                for n in range(HC):
                    last = dve.tensor_scalar(spread[:, 0, n, :], qk_f[:, h, 1, 0, :], mask8[:, n:n + 1], None, ALU.mult)
                last.then_inc(sem("spread1_ready"), 1)

            def score1(h):
                spread1(h)
                for t in tiles(h):
                    dve.wait_ge(sem(f"rel_in{t}"), 32)
                    view = sc[0:ROWS, t].rearrange("p k h -> p h k")
                    for c in range(KD):
                        dve.wait_ge(sem("s1_full"), 2 * t + c + 1)
                        part = view[:, c * HC:(c + 1) * HC, :]
                        dve.tensor_tensor(part, bank("s1", 2 * t + c)[0:ROWS, 0:HC * L].rearrange("p (h k) -> p h k", h=HC),
                                          part, ALU.add).then_inc(sem("ss_ready"), 1)
                    dve.wait_ge(sem("ss_ready"), 2 * t + 2)
                    dve.tensor_reduce(top[0:ROWS, t, :], view, AX.X, ALU.max).then_inc(sem("top_ready"), 1)

            def sum1(h):
                def by_head(t):
                    dve.wait_ge(sem("p_ready"), t + 1)
                    if t >= 2:
                        dve.wait_ge(sem("pt_full"), 2 * t - 2)
                    dve.tensor_copy(ph[0:ROWS, t % 2].rearrange("p (h k) -> p h k", k=L),
                                    sc[0:ROWS, t].rearrange("p k h -> p h k")).then_inc(sem("ph_ready"), 1)

                by_head(NT * h)
                by_head(NT * h + 1)
                for t in tiles(h):
                    if t + 2 < NT * (h + 1):
                        by_head(t + 2)
                    dve.wait_ge(sem("pv1_full"), t + 1)
                    sums = bank("pv1", t)[0:ROWS, 0:H * VW].rearrange("p (a h e) -> p a h e", a=1, h=H)
                    divide(sums, t * H, xn[0:ROWS, t:t + 1, :].rearrange("p t (h e) -> p t h e", h=H), "a1_ready")

            def out1(h):
                add_residual("o1", "h3_ready", h)

            def norm3(h):
                dve.wait_ge(sem("h3_ready"), 2 * (h + 1))
                norm(3, h)

            def ffn1(h):
                for t in tiles(h):
                    dve.wait_ge(sem("fa_full"), t + 1)
                    last = dve.tensor_tensor(logit[0:ROWS, t, :], bank("fa", t)[0:ROWS, FA - EXPERTS:FA], row("router_b")[0:ROWS],
                                             ALU.add)
                link(last)
                for t in tiles(h):
                    last = dve.max(best[0:ROWS, t, :], logit[0:ROWS, t, :])
                link(last)
                ts = slice(NT * h, NT * h + NT)
                dve.tensor_tensor(shifted[0:ROWS, ts, :], logit[0:ROWS, ts, :],
                                  best[0:ROWS, ts, 0:1].to_broadcast([ROWS, NT, EXPERTS]), ALU.subtract)\
                    .then_inc(sem("lshift_ready"), 1)
                link(dve.tensor_tensor(gate[0:ROWS, ts, :], logit[0:ROWS, ts, :],
                                       best[0:ROWS, ts, 1:2].to_broadcast([ROWS, NT, EXPERTS]), ALU.is_ge))
                dve.wait_ge(sem("expo_ready"), h + 1)
                link(dve.tensor_tensor(gate[0:ROWS, ts, :], gate[0:ROWS, ts, :], expo[0:ROWS, ts, :], ALU.mult))
                link(dve.tensor_reduce(gsum[0:ROWS, ts], gate[0:ROWS, ts, :], AX.X, ALU.add))
                link(dve.reciprocal(gsum[0:ROWS, ts], gsum[0:ROWS, ts]))
                link(dve.tensor_scalar(gsum[0:ROWS, ts], gsum[0:ROWS, ts], LORA_SCALE, None, ALU.mult))
                link(dve.tensor_tensor(gate[0:ROWS, ts, :], gate[0:ROWS, ts, :],
                                       gsum[0:ROWS, ts].unsqueeze(2).to_broadcast([ROWS, NT, EXPERTS]), ALU.mult))
                if h == 1:
                    dve.wait_ge(sem("wt_full"), 1)
                for n, t in enumerate(tiles(h)):
                    last = dve.tensor_tensor(wax[0:ROWS, n, :].rearrange("p (e r) -> p e r", r=RANK),
                                             bank("fa", t)[0:ROWS, D:D + EXPERTS * RANK].rearrange("p (e r) -> p e r", r=RANK),
                                             gate[0:ROWS, t, :].unsqueeze(2).to_broadcast([ROWS, EXPERTS, RANK]), ALU.mult)
                last.then_inc(sem("wax_ready"), 1)
                dve.wait_ge(sem("res_final"), h + 1)
                for t in tiles(h):
                    dve.wait_ge(sem("fb_full"), t + 1)
                    dve.tensor_tensor(xn[0:ROWS, t, :], bank("fa", t)[0:ROWS, 0:D], res[0:ROWS, t, :], ALU.add)\
                        .then_inc(sem("out_ready"), 1)

            def weights(h):
                dve.wait_ge(sem("wsum_full"), 1)
                link(dve.tensor_scalar(wscale[:, :], bank("wsum", 0)[:, 0:2], 1.0 / (D * HID), QUANT_EPS, ALU.mult, ALU.max))
                link(dve.reciprocal(winv[:, :], wscale[:, :]))
                dve.tensor_scalar(wscale_127[:, :], wscale[:, :], 1.0 / QMAX, None, ALU.mult).then_inc(sem("wscale_ready"), 1)

            dve_stages = {"embed": embed, "norm0": norm0, "weights": weights, "proj0": proj0, "score0": score0, "sum0": sum0, "out0": out0,
                          "norm1": norm1, "conv": conv, "ffn0": ffn0, "norm2": norm2, "proj1": proj1, "score1": score1, "sum1": sum1,
                          "out1": out1, "norm3": norm3, "ffn1": ffn1}
            for stage, h in ORDER:
                if stage in dve_stages:
                    dve_stages[stage](h)


def _chunks(w):
    return np.ascontiguousarray(w.reshape(-1, P, w.shape[1]).transpose(1, 0, 2))


def _token_rows():
    f = np.float32
    c = np.zeros((P, NCONST), f)

    def put(name, rows, value):
        a, n = CONST[name]
        c[0:rows, a:a + n] = value

    p = np.arange(P)
    put("ident", P, np.eye(P, dtype=f))
    put("mask8", P, p[:, None] // E == np.arange(HC)[None, :])
    third = np.array([(h % HC) % 3 for h in range(H)])
    put("mask3", G3, p[:G3, None] // L == third[None, :])
    m = np.zeros((ROWS, L), f)
    for b in range(2):
        m[SLOT * b:SLOT * b + L] = np.triu(np.ones((L, L), f))
    put("causal", ROWS, m)
    inv = (f(1.0) / f(10000.0) ** (np.arange(0, E, 2, dtype=f) / f(E))).astype(f)
    ang = np.outer(np.arange(L, dtype=f), inv).astype(f)
    cos, sin = np.cos(ang).astype(f).T, np.sin(ang).astype(f).T
    pair = (p % E) // 2
    sign = np.where(p % 2 == 0, f(-1), f(1))[:, None]
    put("cos_k", P, cos[pair])
    put("sin_k", P, sign * sin[pair])
    scale = f(1.0 / np.sqrt(E))
    put("cos_q", P, scale * cos[pair])
    put("sin_q", P, scale * sign * sin[pair])
    return c


def kernel(x, L0_tok_W, L0_tok_b, L0_tok_pos_embd, L0_attn_qkv_w, L0_attn_qkv_b, L0_attn_out_w, L0_attn_out_b,
           L0_ffn_w1, L0_ffn_conv_w, L0_ffn_conv_b, L0_ffn_w2, L1_attn_w_q, L1_attn_w_k, L1_attn_w_v, L1_attn_w_o,
           L1_attn_rel_emb, L1_ffn_base_w, L1_ffn_base_b, L1_ffn_lora_A, L1_ffn_lora_B, L1_ffn_router_w,
           L1_ffn_router_b):
    import concourse.bacc as _bacc
    from concourse.bass_utils import run_bass_kernel_spmd as _run

    a = np.asarray
    patches = a(x).reshape(B, 3, 6, 16, 6, 16).transpose(1, 3, 5, 0, 2, 4).reshape(PATCH, B * L)
    rel = a(L1_attn_rel_emb)
    index = np.maximum(np.arange(L) - (L - 1), -(rel.shape[0] // 2)) + rel.shape[0] // 2
    rel = rel[index]
    cols = np.zeros((P, NCOLS), np.float32)

    def put(name, rows, value):
        at, n = COLS[name]
        cols[0:rows, at:at + n] = value

    put("tok_b", P, a(L0_tok_b).reshape(KD, P).T)
    put("qk_b", P, a(L0_attn_qkv_b)[:2 * D].reshape(2 * KD, P).T)
    put("conv_w", P, a(L0_ffn_conv_w).reshape(MH, P, 3).transpose(1, 0, 2).reshape(P, 3 * MH))
    put("conv_b", P, a(L0_ffn_conv_b).reshape(MH, P).T)
    put("rel_q", P, np.tile(rel.T, (HC, 1)))
    put("rel_v", G3, np.tile(rel, (3, 1)))
    rows = np.concatenate([a(L0_attn_qkv_b)[2 * D:], a(L0_attn_out_b), a(L1_ffn_base_b), a(L1_ffn_router_b)])[None, :]
    lora_a = a(L1_ffn_lora_A).transpose(1, 0, 2).reshape(D, EXPERTS * RANK)
    arrays = {
        "x": _chunks(patches),
        "tok_w": _chunks(a(L0_tok_W).T),
        "pos": np.ascontiguousarray(a(L0_tok_pos_embd)[0].T.reshape(KD, P, L).transpose(1, 0, 2)),
        "cols": cols,
        "rows": np.ascontiguousarray(rows),
        "const": _token_rows(),
        "qkv0_w": _chunks(a(L0_attn_qkv_w).T),
        "o0_w": _chunks(a(L0_attn_out_w).T),
        "w1": _chunks(a(L0_ffn_w1).T).reshape(P, KD * HID),
        "w2": _chunks(a(L0_ffn_w2).T).reshape(P, MH * D),
        "qkv1_w": _chunks(np.concatenate([a(L1_attn_w_q).T, a(L1_attn_w_k).T, a(L1_attn_w_v).T], axis=1)),
        "o1_w": _chunks(a(L1_attn_w_o).T),
        "ffn1_w": _chunks(np.concatenate([a(L1_ffn_base_w).T, lora_a, a(L1_ffn_router_w).T], axis=1)),
        "lora_b": np.ascontiguousarray(a(L1_ffn_lora_B).reshape(EXPERTS * RANK, D)),
    }
    nc = _bacc.Bacc("TRN2", target_bir_lowering=False, num_devices=1)
    feeds, args = {}, []
    for name, v in arrays.items():
        feeds["in_" + name] = v
        args.append(nc.dram_tensor("in_" + name, v.shape, mybir.dt.from_np(v.dtype), kind="ExternalInput").ap())
    args.append(nc.dram_tensor("out_tower", (B, L, D), F32, kind="ExternalOutput").ap())
    build(nc, *args)
    r = _run(nc, [feeds], core_ids=[0])
    return r.results[0]["out_tower"]
```
